# Optimizing a Trainium2 kernel written in Bass

```python
import numpy as np
import jax
import jax.numpy as jnp

def _softmax(x, axis=-1):
    return jax.nn.softmax(x, axis=axis)

def _gelu(x):
    return jax.nn.gelu(x, approximate=True)

def _silu(x):
    return jax.nn.silu(x)

def _sigmoid(x):
    return jax.nn.sigmoid(x)

def _layernorm(x, axis=-1, eps=1e-05):
    m = jnp.mean(x, axis=axis, keepdims=True)
    v = jnp.var(x, axis=axis, keepdims=True)
    return (x - m) / jnp.sqrt(v + eps)

def _scatter_add(tgt, idx, src, axis=0):
    return tgt.at[idx].add(src)

def _segment_sum(src, seg, n):
    return jax.ops.segment_sum(src, seg, n)
kernel_name = 'mk_rec_standalone_d1_rec_r8_114307'

def setup_inputs(seed: int=0):
    np.random.seed(seed)
    _w = jnp.asarray

    def _rec_inputs():
        import jax
        import jax.numpy as jnp
        _rk = jax.random.key(seed)
        r_ds_input = -0.00338568 + 1.0005 * jax.random.normal(jax.random.fold_in(_rk, 1), (2048, 13), jnp.float32)
        r_sp_input = jnp.stack([jax.random.randint(jax.random.fold_in(jax.random.fold_in(_rk, 2), 0), (2048,), 2, 12500, jnp.int32), jax.random.randint(jax.random.fold_in(jax.random.fold_in(_rk, 2), 1), (2048,), 1, 99999, jnp.int32), jax.random.randint(jax.random.fold_in(jax.random.fold_in(_rk, 2), 2), (2048,), 0, 12500, jnp.int32), jax.random.randint(jax.random.fold_in(jax.random.fold_in(_rk, 2), 3), (2048,), 5, 12500, jnp.int32), jax.random.randint(jax.random.fold_in(jax.random.fold_in(_rk, 2), 4), (2048,), 20, 99993, jnp.int32), jax.random.randint(jax.random.fold_in(jax.random.fold_in(_rk, 2), 5), (2048,), 0, 99993, jnp.int32), jax.random.randint(jax.random.fold_in(jax.random.fold_in(_rk, 2), 6), (2048,), 2, 99999, jnp.int32), jax.random.randint(jax.random.fold_in(jax.random.fold_in(_rk, 2), 7), (2048,), 2, 99995, jnp.int32), jax.random.randint(jax.random.fold_in(jax.random.fold_in(_rk, 2), 8), (2048,), 0, 99999, jnp.int32), jax.random.randint(jax.random.fold_in(jax.random.fold_in(_rk, 2), 9), (2048,), 2, 99986, jnp.int32), jax.random.randint(jax.random.fold_in(jax.random.fold_in(_rk, 2), 10), (2048,), 4, 99999, jnp.int32), jax.random.randint(jax.random.fold_in(jax.random.fold_in(_rk, 2), 11), (2048,), 15, 99999, jnp.int32), jax.random.randint(jax.random.fold_in(jax.random.fold_in(_rk, 2), 12), (2048,), 0, 99989, jnp.int32), jax.random.randint(jax.random.fold_in(jax.random.fold_in(_rk, 2), 13), (2048,), 5, 99990, jnp.int32), jax.random.randint(jax.random.fold_in(jax.random.fold_in(_rk, 2), 14), (2048,), 2, 99996, jnp.int32), jax.random.randint(jax.random.fold_in(jax.random.fold_in(_rk, 2), 15), (2048,), 3, 99994, jnp.int32), jax.random.randint(jax.random.fold_in(jax.random.fold_in(_rk, 2), 16), (2048,), 0, 99998, jnp.int32), jax.random.randint(jax.random.fold_in(jax.random.fold_in(_rk, 2), 17), (2048,), 13, 99998, jnp.int32), jax.random.randint(jax.random.fold_in(jax.random.fold_in(_rk, 2), 18), (2048,), 10, 12498, jnp.int32), jax.random.randint(jax.random.fold_in(jax.random.fold_in(_rk, 2), 19), (2048,), 0, 99999, jnp.int32), jax.random.randint(jax.random.fold_in(jax.random.fold_in(_rk, 2), 20), (2048,), 0, 99995, jnp.int32), jax.random.randint(jax.random.fold_in(jax.random.fold_in(_rk, 2), 21), (2048,), 1, 99998, jnp.int32), jax.random.randint(jax.random.fold_in(jax.random.fold_in(_rk, 2), 22), (2048,), 1, 99997, jnp.int32), jax.random.randint(jax.random.fold_in(jax.random.fold_in(_rk, 2), 23), (2048,), 2, 99989, jnp.int32), jax.random.randint(jax.random.fold_in(jax.random.fold_in(_rk, 2), 24), (2048,), 6, 12500, jnp.int32), jax.random.randint(jax.random.fold_in(jax.random.fold_in(_rk, 2), 25), (2048,), 2, 99995, jnp.int32)], axis=1)
        return (r_ds_input, r_sp_input)
    r_ds_input, r_sp_input = _rec_inputs()

    def _L0_rec_setup():
        import jax, jax.numpy as jnp
        import numpy as np
        B = 2048
        DS_DIM = 13
        SP_DIM = 26
        NUM_CATS = 12500
        EMBED_DIM = 32
        HID = [256, 128]
        key = jax.random.key(seed)
        ks = jax.random.split(key, 12)
        ds_input = jax.random.normal(ks[0], (B, DS_DIM), dtype=jnp.float32)
        sp_input = jax.random.randint(ks[1], (B, SP_DIM), 0, NUM_CATS, dtype=jnp.int64)
        xav = float(np.sqrt(2.0 / (NUM_CATS + EMBED_DIM)))
        emb_tables = jax.random.normal(ks[2], (SP_DIM, NUM_CATS, EMBED_DIM), dtype=jnp.float32) * xav
        lin_tables = jax.random.normal(ks[3], (SP_DIM, NUM_CATS, 1), dtype=jnp.float32) * 0.02
        lin_w = jax.random.normal(ks[4], (1, DS_DIM), dtype=jnp.float32) * 0.1
        lin_b = jnp.zeros((1,), dtype=jnp.float32)
        d0 = EMBED_DIM + DS_DIM
        w1 = jax.random.normal(ks[5], (HID[0], d0), dtype=jnp.float32) * float(np.sqrt(1.0 / d0))
        b1 = jnp.zeros((HID[0],), dtype=jnp.float32)
        w2 = jax.random.normal(ks[6], (HID[1], HID[0]), dtype=jnp.float32) * float(np.sqrt(1.0 / HID[0]))
        b2 = jnp.zeros((HID[1],), dtype=jnp.float32)
        fw = jax.random.normal(ks[7], (1, HID[1]), dtype=jnp.float32) * float(np.sqrt(1.0 / HID[1]))
        fb = jnp.zeros((1,), dtype=jnp.float32)
        return {'ds_input': ds_input, 'sp_input': sp_input, 'emb_tables': emb_tables, 'lin_tables': lin_tables, 'lin_w': lin_w, 'lin_b': lin_b, 'w1': w1, 'b1': b1, 'w2': w2, 'b2': b2, 'fw': fw, 'fb': fb}
    _L0_rec_all = _L0_rec_setup()
    _L0_rec_in = {k: v for k, v in _L0_rec_all.items() if k in ('emb_tables', 'lin_tables', 'lin_w', 'lin_b', 'w1', 'b1', 'w2', 'b2', 'fw', 'fb')}
    del _L0_rec_all
    return {'r_ds_input': r_ds_input, 'r_sp_input': r_sp_input, 'L0_rec_emb_tables': _L0_rec_in['emb_tables'], 'L0_rec_lin_tables': _L0_rec_in['lin_tables'], 'L0_rec_lin_w': _L0_rec_in['lin_w'], 'L0_rec_lin_b': _L0_rec_in['lin_b'], 'L0_rec_w1': _L0_rec_in['w1'], 'L0_rec_b1': _L0_rec_in['b1'], 'L0_rec_w2': _L0_rec_in['w2'], 'L0_rec_b2': _L0_rec_in['b2'], 'L0_rec_fw': _L0_rec_in['fw'], 'L0_rec_fb': _L0_rec_in['fb']}

def reference(r_ds_input, r_sp_input, L0_rec_emb_tables, L0_rec_lin_tables, L0_rec_lin_w, L0_rec_lin_b, L0_rec_w1, L0_rec_b1, L0_rec_w2, L0_rec_b2, L0_rec_fw, L0_rec_fb):
    import jax
    import jax.numpy as jnp

    def _L0_rec_ref(ds_input, sp_input, emb_tables, lin_tables, lin_w, lin_b, w1, b1, w2, b2, fw, fb):
        import jax, jax.numpy as jnp
        import numpy as np
        B = 2048
        DS_DIM = 13
        SP_DIM = 26
        NUM_CATS = 12500
        EMBED_DIM = 32
        HID = [256, 128]
        F = emb_tables.shape[0]
        fidx = jnp.arange(F)[None, :]
        sp_emb = emb_tables[fidx, sp_input]
        lin_vals = lin_tables[fidx, sp_input, 0]
        lin_output = ds_input @ lin_w.T + lin_b + jnp.sum(lin_vals, axis=1, keepdims=True)
        s = jnp.sum(sp_emb, axis=1)
        bi_pooled = 0.5 * (s * s - jnp.sum(sp_emb * sp_emb, axis=1))
        x = jnp.concatenate([bi_pooled, ds_input], axis=1)
        h = jax.nn.relu(x @ w1.T + b1)
        h = jax.nn.relu(h @ w2.T + b2)
        out = jax.nn.sigmoid(h @ fw.T + fb + lin_output)
        return out
    y = _L0_rec_ref(r_ds_input, r_sp_input, L0_rec_emb_tables, L0_rec_lin_tables, L0_rec_lin_w, L0_rec_lin_b, L0_rec_w1, L0_rec_b1, L0_rec_w2, L0_rec_b2, L0_rec_fw, L0_rec_fb)
    return y

_drawn_inputs = setup_inputs


def setup_inputs(seed=0):
    import zlib

    import numpy as np

    out = dict(_drawn_inputs(seed))
    spreads = {'L0_rec_b1': (0.0, 0.356), 'L0_rec_b2': (0.0, 0.1)}
    factors = {'L0_rec_emb_tables': 8.0}
    for name, (base, spread) in spreads.items():
        noise = np.random.default_rng([zlib.crc32(name.encode()), seed]).standard_normal(out[name].shape)
        drawn = base * np.exp(spread * noise) if base else spread * noise
        out[name] = jnp.asarray(drawn.astype(out[name].dtype))
    for name, factor in factors.items():
        out[name] = (out[name] * factor).astype(out[name].dtype)
    return out
```

```python
import concourse.bass as bass
from concourse import mybir
from contextlib import ExitStack


def build_deep_fm(nc, dense, sparse, table, w1x, w2t, b2c, fwc, wlx, out):
    fp32 = mybir.dt.float32
    i32 = mybir.dt.int32
    ALU = mybir.AluOpType
    ACT = mybir.ActivationFunctionType
    AX = mybir.AxisListType

    P = 128
    B, DS = dense.shape
    F = sparse.shape[1]
    CATS = table.shape[0] // F
    W = table.shape[1]
    E = W - 1
    H1 = w1x.shape[1]
    H2 = w2t.shape[1]
    HC = H1 // P
    TILES = B // P
    X = w1x.shape[0]
    LAG = 4

    ctx = ExitStack()
    with ctx:
        def sb(name, shape, dt=fp32):
            return ctx.enter_context(nc.sbuf_tensor(name, shape, dt))

        def pb(name, shape):
            return ctx.enter_context(nc.psum_tensor(name, shape, fp32))

        def sem(name):
            return ctx.enter_context(nc.semaphore(name))

        idx_raw = sb("idx_raw", [P, TILES * F], i32)
        idx_low = sb("idx_low", [P, TILES * F], i32)
        idx_wrap = sb("idx_wrap", [P, TILES * F], i32)
        idx_clip = sb("idx_clip", [P, TILES * F], i32)
        field_base = sb("field_base", [P, TILES, F], i32)
        row_idx = sb("row_idx", [P, TILES * F], i32)
        idx_now = [sb(f"idx_now{k}", [P, F], i32) for k in range(LAG)]
        rows = [sb(f"rows{k}", [P, F * W]) for k in range(LAG)]
        squares = sb("squares", [P, LAG, F * E])
        sum_sq = sb("sum_sq", [P, LAG, E])
        sum_emb = sb("sum_emb", [P, LAG, W])
        half_sq = sb("half_sq", [P, LAG, E])
        dense_sb = sb("dense_sb", [P, TILES * DS])
        x = sb("x", [P, LAG, P])
        xT = sb("xT", [X, LAG, P])
        h1 = sb("h1", [P, LAG, HC * P])
        h2 = sb("h2", [P, LAG, P])
        y = sb("y", [P, TILES])
        ident = sb("ident", [P, P])
        w1_sb = sb("w1_sb", [X, H1])
        w2_sb = sb("w2_sb", [P, HC, H2])
        b2_sb = sb("b2_sb", [H2, 1])
        fw_sb = sb("fw_sb", [H2, 1])
        wl_sb = sb("wl_sb", [X, 1])

        xT_ps = [pb(f"xT_ps{i}", [P, P]) for i in range(2)]
        h1_ps = [pb(f"h1_ps{i}", [P, HC * P]) for i in range(2)]
        h2_ps = [pb(f"h2_ps{i}", [H2, P]) for i in range(2)]
        y_ps = [pb(f"y_ps{i}", [P, 1]) for i in range(2)]

        idx_in = sem("idx_in")
        dense_in = sem("dense_in")
        weights_in = sem("weights_in")
        base_made = sem("base_made")
        ident_made = sem("ident_made")
        idx_step = sem("idx_step")
        idx_set = sem("idx_set")
        gathered = [sem(f"gathered{k}") for k in range(LAG)]
        squared = sem("squared")
        reduced = sem("reduced")
        x_fixed = sem("x_fixed")
        pooled_half = sem("pooled_half")
        x_made = sem("x_made")
        xT_done = sem("xT_done")
        xT_copied = sem("xT_copied")
        h1_done = sem("h1_done")
        h1_made = sem("h1_made")
        h2_done = sem("h2_done")
        h2_made = sem("h2_made")
        y_done = sem("y_done")
        y_made = sem("y_made")
        stored = sem("stored")

        block = ctx.enter_context(nc.Block())

        @block.sync
        def _(sp):
            sp.dma_start(idx_raw[:, :], sparse.rearrange("(p t) f -> p (t f)", p=P)).then_inc(idx_in, 16)
            sp.dma_start(dense_sb[:, :], dense.rearrange("(p t) d -> p (t d)", p=P)).then_inc(dense_in, 16)
            sp.dma_start(w1_sb[:, :], w1x).then_inc(weights_in, 16)
            sp.dma_start(w2_sb[:, :, :], w2t.rearrange("(c p) n -> p c n", p=P)).then_inc(weights_in, 16)
            sp.dma_start(b2_sb[:, :], b2c).then_inc(weights_in, 16)
            sp.dma_start(fw_sb[:, :], fwc).then_inc(weights_in, 16)
            sp.dma_start(wl_sb[:, :], wlx).then_inc(weights_in, 16)
            sp.wait_ge(y_made, TILES)
            sp.dma_start(out.rearrange("(p t) o -> p (t o)", p=P), y[:, :]).then_inc(stored, 16)
            sp.wait_ge(stored, 16)

        @block.gpsimd
        def _(pool):
            pool.iota(field_base[:, :, :], pattern=[[0, TILES], [CATS, F]], base=0,
                      channel_multiplier=0).then_inc(base_made, 1)
            pool.memset(ident[:, :], 0.0).then_inc(ident_made, 1)
            pool.wait_ge(ident_made, 1)
            pool.affine_select(out=ident[:, :], in_=ident[:, :], compare_op=ALU.not_equal, fill=1.0,
                               base=0, pattern=[[-1, P]], channel_multiplier=1).then_inc(ident_made, 1)
            with pool.Fori(0, TILES // LAG) as g:
                for k in range(LAG):
                    pool.wait_ge(idx_set, g * LAG + (k + 1))
                    pool.nop(nofuse=True)
                    for f in range(F):
                        pool.indirect_dma_start(
                            out=rows[k][:, f * W:(f + 1) * W], out_offset=None,
                            in_=table[:, :],
                            in_offset=bass.IndirectOffsetOnAxis(ap=idx_now[k][:, f:f + 1], axis=0),
                        ).then_inc(gathered[k], 16)

        @block.vector
        def _(dve):
            dve.wait_ge(idx_in, 16)
            nc.vector.tensor_scalar(idx_low[:, :], idx_raw[:, :], CATS - 1, None, ALU.min).then_inc(idx_step, 1)
            dve.wait_ge(idx_step, 1)
            nc.vector.tensor_scalar(idx_wrap[:, :], idx_low[:, :], 0, CATS, ALU.is_lt, ALU.mult).then_inc(idx_step, 1)
            dve.wait_ge(idx_step, 2)
            nc.vector.tensor_tensor(idx_clip[:, :], idx_low[:, :], idx_wrap[:, :], ALU.add).then_inc(idx_step, 1)
            dve.wait_ge(idx_step, 3)
            dve.wait_ge(base_made, 1)
            nc.vector.scalar_tensor_tensor(
                row_idx[:, :], idx_clip[:, :], 0, field_base[:, :, :].rearrange("p t f -> p (t f)"),
                ALU.max, ALU.add).then_inc(idx_step, 1)
            dve.wait_ge(idx_step, 4)
            for k in range(LAG):
                nc.vector.tensor_copy(idx_now[k][:, :], row_idx[:, k * F:(k + 1) * F]).then_inc(idx_set, 1)
            dve.wait_ge(dense_in, 16)
            nc.vector.memset(x[:, :, :], 1.0).then_inc(x_fixed, 1)

            def tile(g, k, set_next=True):
                t = g * LAG + k
                dve.wait_ge(gathered[k], (g + 1) * (16 * F))
                nc.vector.tensor_reduce(
                    sum_emb[:, k, :], rows[k][:, :].rearrange("p (f w) -> p w f", w=W),
                    AX.X, ALU.add).then_inc(reduced, 1)
                dve.wait_ge(squared, t + 1)
                nc.vector.tensor_reduce(
                    sum_sq[:, k, :], squares[:, k, :].rearrange("p (f e) -> p e f", e=E),
                    AX.X, ALU.add).then_inc(reduced, 1)
                dve.wait_ge(reduced, 2 * t + 2)
                if set_next:
                    nc.vector.tensor_copy(idx_now[k][:, :],
                                          row_idx[:, bass.ds((t + LAG) * F, F)]).then_inc(idx_set, 1)
                nc.vector.tensor_copy(x[:, k, E:W], sum_emb[:, k, E:W])
                nc.vector.tensor_copy(x[:, k, W:W + DS], dense_sb[:, bass.ds(t * DS, DS)])
                nc.vector.scalar_tensor_tensor(half_sq[:, k, :], sum_emb[:, k, 0:E], 0.5, sum_emb[:, k, 0:E],
                                               ALU.mult, ALU.mult).then_inc(pooled_half, 1)
                dve.wait_ge(pooled_half, t + 1)
                nc.vector.scalar_tensor_tensor(x[:, k, 0:E], sum_sq[:, k, :], -0.5, half_sq[:, k, :],
                                               ALU.mult, ALU.add).then_inc(x_made, 1)
                dve.wait_ge(xT_done, t + 1)
                nc.vector.tensor_copy(xT[:, k, :], xT_ps[k % 2][0:X, :]).then_inc(xT_copied, 1)

            with dve.Fori(0, TILES // LAG - 1) as g:
                for k in range(LAG):
                    tile(g, k)
            for k in range(LAG):
                tile(TILES // LAG - 1, k, set_next=False)

        @block.scalar
        def _(act):
            act.wait_ge(weights_in, 16 * 5)

            def tile(g, k):
                t = g * LAG + k
                act.wait_ge(gathered[k], (g + 1) * (16 * F))
                nc.scalar.activation(
                    squares[:, k, :].rearrange("p (f e) -> p f e", e=E),
                    rows[k][:, :].rearrange("p (f w) -> p f w", w=W)[:, :, 0:E],
                    ACT.Square).then_inc(squared, 1)
                act.wait_ge(h1_done, t + 1)
                nc.scalar.activation(h1[:, k, :], h1_ps[k % 2][:, :], ACT.Relu).then_inc(h1_made, 1)
                act.wait_ge(h2_done, t + 1)
                nc.scalar.activation(h2[:, k, :], h2_ps[k % 2][:, :], ACT.Relu, bias=b2_sb[:, 0:1]).then_inc(h2_made, 1)
                act.wait_ge(y_done, t + 1)
                nc.scalar.activation(y[:, bass.ds(t, 1)], y_ps[k % 2][:, :], ACT.Sigmoid).then_inc(y_made, 1)

            with act.Fori(0, TILES // LAG) as g:
                for k in range(LAG):
                    tile(g, k)

        @block.tensor
        def _(pe):
            pe.wait_ge(ident_made, 2)
            pe.wait_ge(weights_in, 16 * 5)

            def tile(g, k):
                t = g * LAG + k
                pe.wait_ge(x_fixed, 1)
                pe.wait_ge(x_made, t + 1)
                nc.tensor.transpose(xT_ps[k % 2][:, :], x[:, k, :], ident[:, :]).then_inc(xT_done, 1)
                pe.wait_ge(xT_copied, t + 1)
                for c in range(HC):
                    last = nc.tensor.matmul(h1_ps[k % 2][:, c * P:(c + 1) * P], w1_sb[:, c * P:(c + 1) * P],
                                            xT[:, k, :], start=True, stop=True)
                last.then_inc(h1_done, 1)
                pe.wait_ge(h1_made, t + 1)
                for c in range(HC):
                    last = nc.tensor.matmul(h2_ps[k % 2][:, :], w2_sb[:, c, :], h1[:, k, c * P:(c + 1) * P],
                                            start=(c == 0), stop=(c == HC - 1))
                last.then_inc(h2_done, 1)
                nc.tensor.matmul(y_ps[k % 2][:, :], xT[:, k, :], wl_sb[:, :], start=True, stop=False)
                pe.wait_ge(h2_made, t + 1)
                nc.tensor.matmul(y_ps[k % 2][:, :], h2[:, k, :], fw_sb[:, :], start=False, stop=True).then_inc(y_done, 1)

            with pe.Fori(0, TILES // LAG) as g:
                for k in range(LAG):
                    tile(g, k)


def kernel(r_ds_input, r_sp_input, L0_rec_emb_tables, L0_rec_lin_tables, L0_rec_lin_w, L0_rec_lin_b,
           L0_rec_w1, L0_rec_b1, L0_rec_w2, L0_rec_b2, L0_rec_fw, L0_rec_fb):
    import numpy as np
    import concourse.bacc as bacc
    from concourse.bass_utils import run_bass_kernel_spmd

    ds, sp, emb, lin, lin_w, lin_b, w1, b1, w2, b2, fw, fb = (np.asarray(a) for a in (
        r_ds_input, r_sp_input, L0_rec_emb_tables, L0_rec_lin_tables, L0_rec_lin_w, L0_rec_lin_b,
        L0_rec_w1, L0_rec_b1, L0_rec_w2, L0_rec_b2, L0_rec_fw, L0_rec_fb))
    F, C, E = emb.shape
    H1, H2 = w1.shape[0], w2.shape[0]
    zero = np.zeros((1, H1), w1.dtype)
    one = np.ones((1, 1), w1.dtype)
    arrays = {
        "dense": ds,
        "sparse": sp,
        "table": np.concatenate([emb, lin], axis=2).reshape(F * C, E + 1),
        "w1x": np.concatenate([w1.T[:E], zero, w1.T[E:], b1.reshape(1, H1), zero], axis=0),
        "w2t": np.ascontiguousarray(w2.T),
        "b2c": b2.reshape(H2, 1),
        "fwc": fw.reshape(H2, 1),
        "wlx": np.concatenate([zero.reshape(H1, 1)[:E], one, lin_w.T, lin_b.reshape(1, 1), fb.reshape(1, 1)], axis=0),
    }
    nc = bacc.Bacc("TRN2", target_bir_lowering=False, num_devices=1)
    aps = [nc.dram_tensor(n, a.shape, mybir.dt.from_np(a.dtype), kind="ExternalInput").ap()
           for n, a in arrays.items()]
    out = nc.dram_tensor("out", (ds.shape[0], 1), mybir.dt.float32, kind="ExternalOutput").ap()
    build_deep_fm(nc, *aps, out)
    return run_bass_kernel_spmd(nc, [arrays], core_ids=[0]).results[0]["out"]
```

```python
import concourse.bass as bass
from concourse import mybir
from contextlib import ExitStack


def build_deep_fm(nc, dense, sparse, cols, table, tabs, w1x, w2t, b2c, fwc, wlx, out):
    fp32 = mybir.dt.float32
    bf16 = mybir.dt.bfloat16
    i32 = mybir.dt.int32
    ALU = mybir.AluOpType
    ACT = mybir.ActivationFunctionType
    AX = mybir.AxisListType

    P = 128
    B, DS = dense.shape
    F = sparse.shape[1]
    CATS = table.shape[0] // F
    W = table.shape[1]
    E = W - 1
    H1 = w1x.shape[1]
    H2 = w2t.shape[1]
    HC = H1 // P
    TILES = B // P
    X = w1x.shape[0]
    MMF = tabs.shape[0]
    GF = F - MMF
    TW = tabs.shape[2]
    J = P // E
    HIS = TW // W
    CHUNKS = HIS // J
    TB = 4
    BLOCKS = TILES // TB
    N = TB * P
    LO_BITS = 7
    J_BITS = 2
    GROUP = 5
    GROUPS = CHUNKS // GROUP
    SUB, HI = range(2)
    assert J == 1 << J_BITS and P == 1 << LO_BITS and CHUNKS % GROUP == 0 and MMF == 4

    codes_dram = nc.dram_tensor("codes_dram", (2, MMF * TILES, P), bf16).ap()

    ctx = ExitStack()
    with ctx:
        def sb(name, shape, dt=fp32):
            return ctx.enter_context(nc.sbuf_tensor(name, shape, dt))

        def pb(name, shape, dt=fp32):
            return ctx.enter_context(nc.psum_tensor(name, shape, dt))

        def sem(name):
            return ctx.enter_context(nc.semaphore(name))

        idx_raw = sb("idx_raw", [P, TILES * F], i32)
        idx_low = sb("idx_low", [P, TILES * F], i32)
        idx_wrap = sb("idx_wrap", [P, TILES * F], i32)
        field_base = sb("field_base", [P, TILES, F], i32)
        row_idx = sb("row_idx", [P, TILES * F], i32)
        idx_now = [sb(f"idx_now{k}", [P, GF], i32) for k in range(TB)]
        rows = [sb(f"rows{k}", [P, GF * W]) for k in range(TB)]
        squares = sb("squares", [P, GF * E])
        g_sum = sb("g_sum", [P, TB, W])
        g_sq = sb("g_sq", [P, TB, E])
        CR = MMF * TILES
        col_raw = sb("col_raw", [CR, P], i32)
        col_low = sb("col_low", [CR, P], i32)
        col_wrap = sb("col_wrap", [CR, P], i32)
        col_clip = sb("col_clip", [CR, P], i32)
        col_bits = sb("col_bits", [CR, 2, P], i32)
        col_code = sb("col_code", [CR, 2, P], bf16)
        codes = [sb(f"codes{n}", [P, 2, N], bf16) for n in range(MMF)]
        mm_clip = sb("mm_clip", [P, MMF, TILES], i32)
        lo_i = sb("lo_i", [P, MMF * TILES], i32)
        chunk_i = sb("chunk_i", [P, MMF * TILES], i32)
        lo_of = sb("lo_of", [P, MMF * TILES])
        chunk_of = sb("chunk_of", [P, MMF * TILES])
        column_i = sb("column_i", [P, P], i32)
        column = sb("column", [P, P], bf16)
        ident_bf = sb("ident_bf", [P, P], bf16)
        whereT = sb("whereT", [P, 2, N], bf16)
        part_i = sb("part_i", [P, 1], i32)
        sub_i = sb("sub_i", [P, 1], i32)
        part_id = sb("part_id", [P, 1])
        sub_id = sb("sub_id", [P, 1])
        stage = [sb(f"stage{k}", [P, TW]) for k in range(2)]
        part = [[sb(f"part{s}_{n}", [P, TW], bf16) for n in range(MMF)] for s in range(3)]
        gates = sb("gates", [P, CHUNKS + 1, N], bf16)
        picked_emb = sb("picked_emb", [P, N])
        picked_lin = sb("picked_lin", [HIS, N])
        picked_sq = sb("picked_sq", [P, N])
        emb_acc = sb("emb_acc", [P, N])
        lin_acc = sb("lin_acc", [HIS, N])
        sq_acc = sb("sq_acc", [P, N])
        dense_sb = sb("dense_sb", [P, TILES * DS])
        sum_all = sb("sum_all", [P, TB, W])
        sq_all = sb("sq_all", [P, TB, E])
        half_sq = sb("half_sq", [P, TB, E])
        x = sb("x", [P, TB, P])
        xT = sb("xT", [X, N])
        h1 = sb("h1", [P, HC, N])
        h2 = sb("h2", [P, N])
        y = sb("y", [P, TILES])
        ident = sb("ident", [P, P])
        fold = sb("fold", [P, E])
        ones = sb("ones", [P, 1])
        w1_sb = sb("w1_sb", [X, H1])
        w2_sb = sb("w2_sb", [P, HC, H2])
        b2_sb = sb("b2_sb", [H2, 1])
        fw_sb = sb("fw_sb", [H2, 1])
        wl_sb = sb("wl_sb", [X, 1])

        cand = [pb(f"cand{k}", [P, N]) for k in range(2)]
        lin_cand = pb("lin_cand", [P, N])
        where = [pb(f"where{k}", [P, 2 * N], bf16) for k in range(2)]
        small_ps = pb("small_ps", [P, N])
        xh_ps = pb("xh_ps", [P, N])
        h1_ps = [pb("h1_ps0", [P, N]), small_ps]
        sum_ps = small_ps[:, 0:TB * W].rearrange("p (i w) -> p i w", w=W)
        sq_ps = small_ps[:, TB * W:TB * (W + E)].rearrange("p (i e) -> p i e", e=E)
        y_ps = small_ps[:, TB * (W + E):TB * (W + E + 1)]

        idx_in = sem("idx_in")
        cols_in = sem("cols_in")
        dense_in = sem("dense_in")
        weights_in = sem("weights_in")
        stage_in = [sem(f"stage_in{k}") for k in range(2)]
        codes_out = sem("codes_out")
        codes_in = [sem(f"codes_in{n}") for n in range(MMF)]
        base_made = sem("base_made")
        ident_made = sem("ident_made")
        idx_step = sem("idx_step")
        col_step = sem("col_step")
        id_step = sem("id_step")
        idx_set = sem("idx_set")
        consts_made = sem("consts_made")
        part0_made = sem("part0_made")
        rest1_made = sem("rest1_made")
        part1_made = sem("part1_made")
        part2_made = sem("part2_made")
        gathered = [sem(f"gathered{k}") for k in range(TB)]
        squared = sem("squared")
        reduced = sem("reduced")
        mm_step = sem("mm_step")
        whereT_made = sem("whereT_made")
        where_made = sem("where_made")
        gates_made = sem("gates_made")
        gates_free = sem("gates_free")
        emb_picked = sem("emb_picked")
        cand_free = sem("cand_free")
        picked_squared = sem("picked_squared")
        summed = sem("summed")
        folded = sem("folded")
        totals = sem("totals")
        half_made = sem("half_made")
        x_made = sem("x_made")
        xT_done = sem("xT_done")
        xT_copied = sem("xT_copied")
        h1_done = sem("h1_done")
        h1_made = sem("h1_made")
        h2_done = sem("h2_done")
        h2_made = sem("h2_made")
        y_done = sem("y_done")
        y_made = sem("y_made")
        stored = sem("stored")

        block = ctx.enter_context(nc.Block())

        @block.sync
        def _(sp):
            sp.dma_start(idx_raw[:, :], sparse.rearrange("(p t) f -> p (t f)", p=P)).then_inc(idx_in, 16)
            sp.dma_start(col_raw[:, :], cols).then_inc(cols_in, 16)
            sp.dma_start(dense_sb[:, :], dense.rearrange("(p t) d -> p (t d)", p=P)).then_inc(dense_in, 16)
            sp.wait_ge(col_step, 8)
            sp.dma_start(codes_dram.rearrange("q r p -> r q p"), col_code[:, :, :]).then_inc(codes_out, 16)
            sp.wait_ge(codes_out, 16)

            def load_codes(b, n):
                src = codes_dram[:, bass.ds(b * TB + n * TILES, TB), :].rearrange("q t p -> q (t p)")
                sp.dma_start(codes[n][:, :, :], src.unsqueeze(0).broadcast_to([P, 2, N])).then_inc(codes_in[n], 16)

            for n in range(MMF):
                load_codes(0, n)
            sp.dma_start(w1_sb[:, :], w1x).then_inc(weights_in, 16)
            sp.dma_start(w2_sb[:, :, :], w2t.rearrange("(c p) n -> p c n", p=P)).then_inc(weights_in, 16)
            sp.dma_start(b2_sb[:, :], b2c).then_inc(weights_in, 16)
            sp.dma_start(fw_sb[:, :], fwc).then_inc(weights_in, 16)
            sp.dma_start(wl_sb[:, :], wlx).then_inc(weights_in, 16)
            with sp.Fori(1, BLOCKS) as b:
                for n in range(MMF):
                    sp.wait_ge(cand_free, b * MMF + (n - MMF + 3))
                    load_codes(b, n)
            sp.wait_ge(y_made, BLOCKS)
            sp.dma_start(out.rearrange("(p t) o -> p (t o)", p=P), y[:, :]).then_inc(stored, 16)
            sp.wait_ge(stored, 16)

        @block.gpsimd
        def _(pool):
            pool.iota(field_base[:, :, :], pattern=[[0, TILES], [CATS, F]], base=0,
                      channel_multiplier=0).then_inc(base_made, 1)
            pool.iota(part_i[:, :], pattern=[[0, 1]], base=0, channel_multiplier=1).then_inc(base_made, 1)
            pool.iota(column_i[:, :], pattern=[[1, P]], base=0, channel_multiplier=0).then_inc(base_made, 1)
            pool.memset(ident[:, :], 0.0).then_inc(ident_made, 1)
            pool.wait_ge(ident_made, 1)
            pool.affine_select(out=ident[:, :], in_=ident[:, :], compare_op=ALU.not_equal, fill=1.0,
                               base=0, pattern=[[-1, P]], channel_multiplier=1).then_inc(ident_made, 1)
            with pool.Fori(0, BLOCKS) as b:
                for k in range(TB):
                    pool.wait_ge(idx_set, b * TB + (k + 1))
                    pool.nop(nofuse=True)
                    for f in range(GF):
                        pool.indirect_dma_start(
                            out=rows[k][:, f * W:(f + 1) * W], out_offset=None,
                            in_=table[:, :],
                            in_offset=bass.IndirectOffsetOnAxis(ap=idx_now[k][:, f:f + 1], axis=0),
                        ).then_inc(gathered[k], 16)

        @block.vector
        def _(dve):
            dve.wait_ge(idx_in, 16)
            nc.vector.tensor_scalar(idx_low[:, :], idx_raw[:, :], CATS - 1, None, ALU.min).then_inc(idx_step, 1)
            dve.wait_ge(idx_step, 1)
            nc.vector.tensor_scalar(idx_wrap[:, :], idx_low[:, :], 0, CATS, ALU.is_lt, ALU.mult).then_inc(idx_step, 1)
            dve.wait_ge(idx_step, 2)
            nc.vector.tensor_tensor(idx_wrap[:, :], idx_low[:, :], idx_wrap[:, :], ALU.add).then_inc(idx_step, 1)
            dve.wait_ge(idx_step, 3)
            dve.wait_ge(base_made, 3)
            nc.vector.scalar_tensor_tensor(
                row_idx[:, :], idx_wrap[:, :], 0, field_base[:, :, :].rearrange("p t f -> p (t f)"),
                ALU.max, ALU.add).then_inc(idx_step, 1)
            dve.wait_ge(idx_step, 4)
            for k in range(TB):
                nc.vector.tensor_copy(idx_now[k][:, :], row_idx[:, k * F + MMF:(k + 1) * F]).then_inc(idx_set, 1)

            dve.wait_ge(cols_in, 16)
            nc.vector.tensor_scalar(col_low[:, :], col_raw[:, :], CATS - 1, None, ALU.min).then_inc(col_step, 1)
            dve.wait_ge(col_step, 1)
            nc.vector.tensor_scalar(col_wrap[:, :], col_low[:, :], 0, CATS, ALU.is_lt, ALU.mult).then_inc(col_step, 1)
            dve.wait_ge(col_step, 2)
            nc.vector.tensor_tensor(col_wrap[:, :], col_low[:, :], col_wrap[:, :], ALU.add).then_inc(col_step, 1)
            dve.wait_ge(col_step, 3)
            nc.vector.tensor_scalar(col_clip[:, :], col_wrap[:, :], 0, None, ALU.max).then_inc(col_step, 1)
            dve.wait_ge(col_step, 4)
            nc.vector.tensor_scalar(col_bits[:, SUB, :], col_clip[:, :], LO_BITS, J - 1,
                                    ALU.arith_shift_right, ALU.bitwise_and).then_inc(col_step, 1)
            nc.vector.tensor_scalar(col_bits[:, HI, :], col_clip[:, :], LO_BITS, None,
                                    ALU.arith_shift_right).then_inc(col_step, 1)
            dve.wait_ge(col_step, 6)
            for q in (SUB, HI):
                nc.vector.tensor_copy(col_code[:, q, :], col_bits[:, q, :]).then_inc(col_step, 1)

            nc.vector.tensor_scalar(mm_clip[:, :, :], idx_wrap[:, :].rearrange("p (t f) -> p f t", f=F)[:, 0:MMF, :],
                                    0, None, ALU.max).then_inc(mm_step, 1)
            dve.wait_ge(mm_step, 1)
            mm_flat = mm_clip[:, :, :].rearrange("p n t -> p (n t)")
            nc.vector.tensor_scalar(lo_i[:, :], mm_flat, P - 1, None, ALU.bitwise_and).then_inc(mm_step, 1)
            nc.vector.tensor_scalar(chunk_i[:, :], mm_flat, LO_BITS + J_BITS, None,
                                    ALU.arith_shift_right).then_inc(mm_step, 1)
            dve.wait_ge(mm_step, 3)
            nc.vector.tensor_copy(lo_of[:, :], lo_i[:, :]).then_inc(mm_step, 1)
            nc.vector.tensor_scalar(chunk_of[:, :], chunk_i[:, :], 1, None, ALU.add).then_inc(mm_step, 1)
            nc.vector.tensor_copy(column[:, :], column_i[:, :]).then_inc(mm_step, 1)
            dve.wait_ge(ident_made, 2)
            nc.vector.tensor_copy(ident_bf[:, :], ident[:, :]).then_inc(consts_made, 1)

            nc.vector.tensor_scalar(sub_i[:, :], part_i[:, :], E.bit_length() - 1, None,
                                    ALU.arith_shift_right).then_inc(id_step, 1)
            nc.vector.tensor_copy(part_id[:, :], part_i[:, :]).then_inc(consts_made, 1)
            dve.wait_ge(id_step, 1)
            nc.vector.tensor_copy(sub_id[:, :], sub_i[:, :]).then_inc(consts_made, 1)
            nc.vector.tensor_reduce(fold[:, :], ident[:, :].rearrange("p (j e) -> p e j", j=J), AX.X,
                                    ALU.add).then_inc(consts_made, 1)
            nc.vector.memset(ones[:, :], 1.0).then_inc(consts_made, 1)
            nc.vector.memset(x[:, :, :], 1.0).then_inc(consts_made, 1)
            nc.vector.memset(picked_sq[:, 0:1], 0.0).then_inc(cand_free, 2)
            nc.vector.memset(picked_sq[:, 1:2], 0.0).then_inc(gates_free, GROUPS)

            def rest1(n):
                dve.wait_ge(part0_made, n + 1)
                nc.vector.tensor_tensor(stage[n % 2][:, :], stage[n % 2][:, :], part[0][n][:, :],
                                        ALU.subtract).then_inc(rest1_made, 1)

            def rest2(n):
                dve.wait_ge(part1_made, n + 1)
                nc.vector.tensor_tensor(part[2][n][:, :], stage[n % 2][:, :], part[1][n][:, :],
                                        ALU.subtract).then_inc(part2_made, 1)

            def make_whereT(b, n):
                for i in range(TB):
                    at = bass.ds(b * TB + (n * TILES + i), 1)
                    last = nc.vector.tensor_scalar(whereT[:, n % 2, i * P:(i + 1) * P], column[:, :],
                                                   lo_of[:, at], chunk_of[:, at], ALU.is_equal, ALU.mult)
                last.then_inc(whereT_made, 1)

            def make_gates(b, n):
                j = b * MMF + n
                dve.wait_ge(where_made, j + 1)
                for g in range(GROUPS):
                    dve.wait_ge(gates_free, j * GROUPS + (g + 1))
                    for c in range(g * GROUP, (g + 1) * GROUP):
                        last = nc.vector.tensor_scalar(gates[:, c, :], where[n % 2][:, 0:N], float(c + 1), None,
                                                       ALU.is_equal)
                    if g == GROUPS - 1:
                        last = nc.vector.tensor_scalar(gates[:, CHUNKS, :], where[n % 2][:, 0:N], 0.0, None, ALU.is_gt)
                    last.then_inc(gates_made, 1)

            ADDS = 3 * (MMF - 1)

            def pick(b, n):
                j = b * MMF + n
                dve.wait_ge(gates_free, (j + 2) * GROUPS)
                dve.wait_ge(codes_in[n], (b + 1) * 16)
                if n > 1:
                    dve.wait_ge(summed, b * ADDS + 3 * (n - 1))
                emb, lin = (emb_acc, lin_acc) if n == 0 else (picked_emb, picked_lin)
                nc.vector.scalar_tensor_tensor(emb[:, :], codes[n][:, SUB, :], sub_id[:, 0:1], cand[n % 2][:, :],
                                               ALU.is_equal, ALU.mult).then_inc(emb_picked, 1)
                nc.vector.scalar_tensor_tensor(lin[:, :], codes[n][0:HIS, HI, :], part_id[0:HIS, 0:1],
                                               lin_cand[0:HIS, :], ALU.is_equal, ALU.mult).then_inc(cand_free, 1)
                if n > 0:
                    dve.wait_ge(emb_picked, j + 1)
                    if n == 1:
                        dve.wait_ge(picked_squared, j)
                    nc.vector.tensor_tensor(emb_acc[:, :], emb_acc[:, :], picked_emb[:, :],
                                            ALU.add).then_inc(summed, 1)
                    dve.wait_ge(cand_free, j + 3)
                    nc.vector.tensor_tensor(lin_acc[:, :], lin_acc[:, :], picked_lin[:, :],
                                            ALU.add).then_inc(summed, 1)

            def add_squares(b, n):
                if n > 0:
                    dve.wait_ge(picked_squared, b * MMF + (n + 1))
                    nc.vector.tensor_tensor(sq_acc[:, :], sq_acc[:, :], picked_sq[:, :],
                                            ALU.add).then_inc(summed, 1)

            def sum_tile(b, k, set_next):
                t = b * TB + k
                dve.wait_ge(gathered[k], (b + 1) * (16 * GF))
                nc.vector.tensor_reduce(
                    g_sum[:, k, :], rows[k][:, :].rearrange("p (f w) -> p w f", w=W),
                    AX.X, ALU.add).then_inc(reduced, 1)
                dve.wait_ge(squared, t + 1)
                nc.vector.tensor_reduce(
                    g_sq[:, k, :], squares[:, :].rearrange("p (f e) -> p e f", e=E),
                    AX.X, ALU.add).then_inc(reduced, 1)
                if set_next:
                    dve.wait_ge(reduced, 2 * t + 2)
                    nc.vector.tensor_copy(idx_now[k][:, :],
                                          row_idx[:, bass.ds((t + TB) * F + MMF, GF)]).then_inc(idx_set, 1)

            def pool_block(b):
                dve.wait_ge(folded, b + 1)
                dve.wait_ge(reduced, (b + 1) * (2 * TB))
                nc.vector.tensor_tensor(sum_all[:, :, :], g_sum[:, :, :], sum_ps, ALU.add).then_inc(totals, 1)
                nc.vector.tensor_tensor(sq_all[:, :, :], g_sq[:, :, :], sq_ps, ALU.add).then_inc(totals, 1)
                dve.wait_ge(totals, 2 * b + 2)
                nc.vector.scalar_tensor_tensor(half_sq[:, :, :], sum_all[:, :, 0:E], 0.5, sum_all[:, :, 0:E],
                                               ALU.mult, ALU.mult).then_inc(half_made, 1)
                nc.vector.tensor_copy(x[:, :, E:W], sum_all[:, :, E:W])
                nc.vector.tensor_copy(x[:, :, W:W + DS], dense_sb[:, bass.ds(b * (TB * DS), TB * DS)]
                                      .rearrange("p (i d) -> p i d", d=DS))
                dve.wait_ge(half_made, b + 1)
                nc.vector.scalar_tensor_tensor(x[:, :, 0:E], sq_all[:, :, :], -0.5, half_sq[:, :, :],
                                               ALU.mult, ALU.add).then_inc(x_made, 1)
                dve.wait_ge(xT_done, b + 1)
                nc.vector.tensor_copy(xT[:, :], xh_ps[0:X, :]).then_inc(xT_copied, 1)

            dve.wait_ge(mm_step, 6)
            for n in (0, 1):
                make_whereT(0, n)
            for n in (0, 1):
                rest1(n)
            for n in (0, 1):
                rest2(n)
            make_gates(0, 0)
            for n in (2, 3):
                rest1(n)
            for n in (2, 3):
                rest2(n)
            dve.wait_ge(dense_in, 16)

            def body(b, last):
                for n in range(MMF):
                    if n + 2 < MMF:
                        make_whereT(b, n + 2)
                    elif not last:
                        make_whereT(b + 1, n + 2 - MMF)
                    if n + 1 < MMF:
                        make_gates(b, n + 1)
                    elif not last:
                        make_gates(b + 1, 0)
                    pick(b, n)
                    sum_tile(b, n, not last)
                    add_squares(b, n)
                pool_block(b)

            with dve.Fori(0, BLOCKS - 1) as b:
                body(b, False)
            body(BLOCKS - 1, True)

        @block.scalar
        def _(act):
            def load_table(n):
                act.dma_start(stage[n % 2][:, :], tabs[n, :, :]).then_inc(stage_in[n % 2], 16)

            def part0(n):
                act.wait_ge(stage_in[n % 2], 16 * (n // 2 + 1))
                nc.scalar.copy(part[0][n][:, :], stage[n % 2][:, :]).then_inc(part0_made, 1)

            def part1(n):
                act.wait_ge(rest1_made, n + 1)
                nc.scalar.copy(part[1][n][:, :], stage[n % 2][:, :]).then_inc(part1_made, 1)

            for n in (0, 1):
                load_table(n)
            for n in (0, 1):
                part0(n)
            for n in (0, 1):
                part1(n)
            for n in (2, 3):
                act.wait_ge(part2_made, n - 1)
                load_table(n)
            for n in (2, 3):
                part0(n)
            for n in (2, 3):
                part1(n)
            act.wait_ge(weights_in, 16 * 5)

            with act.Fori(0, BLOCKS) as b:
                for n in range(MMF):
                    act.wait_ge(emb_picked, b * MMF + (n + 1))
                    src, dst = (emb_acc, sq_acc) if n == 0 else (picked_emb, picked_sq)
                    nc.scalar.activation(dst[:, :], src[:, :], ACT.Square).then_inc(picked_squared, 1)
                    act.wait_ge(gathered[n], (b + 1) * (16 * GF))
                    nc.scalar.activation(
                        squares[:, :].rearrange("p (f e) -> p f e", e=E),
                        rows[n][:, :].rearrange("p (f w) -> p f w", w=W)[:, :, 0:E],
                        ACT.Square).then_inc(squared, 1)
                for c in range(HC):
                    act.wait_ge(h1_done, b * HC + (c + 1))
                    nc.scalar.activation(h1[:, c, :], h1_ps[c][:, :], ACT.Relu).then_inc(h1_made, 1)
                act.wait_ge(h2_done, b + 1)
                nc.scalar.activation(h2[:, :], xh_ps[:, :], ACT.Relu, bias=b2_sb[:, 0:1]).then_inc(h2_made, 1)
                act.wait_ge(y_done, b + 1)
                nc.scalar.activation(y[:, bass.ds(b * TB, TB)], y_ps, ACT.Sigmoid).then_inc(y_made, 1)

        @block.tensor
        def _(pe):
            def turn_where(b, n):
                pe.wait_ge(whereT_made, b * MMF + (n + 1))
                for i in range(TB):
                    last = nc.tensor.transpose(where[n % 2][:, i * P:(i + 1) * P],
                                               whereT[:, n % 2, i * P:(i + 1) * P], ident_bf[:, :])
                last.then_inc(where_made, 1)

            def look_up(b, n, last_field=False):
                j = b * MMF + n
                pe.wait_ge(cand_free, j + 1)
                for g in range(GROUPS):
                    pe.wait_ge(gates_made, j * GROUPS + (g + 1))
                    for c in range(g * GROUP, (g + 1) * GROUP):
                        for s in range(3):
                            last = nc.tensor.matmul(cand[n % 2][:, :], part[s][n][:, c * P:(c + 1) * P],
                                                    gates[:, c, :], start=(c == 0 and s == 0),
                                                    stop=(c == CHUNKS - 1 and s == 2))
                    if g < GROUPS - 1:
                        last.then_inc(gates_free, 1)
                    if g == 0 and not last_field:
                        turn_where(b + (n + 1) // MMF, (n + 1) % MMF)
                pe.wait_ge(cand_free, j + 2)
                for s in range(3):
                    last = nc.tensor.matmul(lin_cand[0:HIS, :], part[s][n][:, CHUNKS * P:CHUNKS * P + HIS],
                                            gates[:, CHUNKS, :], start=(s == 0), stop=(s == 2))
                last.then_inc(gates_free, 1)

            def mlp(b):
                pe.wait_ge(summed, (b + 1) * (3 * (MMF - 1)))
                for i in range(TB):
                    t = slice(i * P, (i + 1) * P)
                    nc.tensor.matmul(sum_ps[:, i, 0:E], emb_acc[:, t], fold[:, :], start=True, stop=True)
                    nc.tensor.matmul(sum_ps[:, i, E:W], lin_acc[:, t], ones[0:HIS, :], start=True, stop=True)
                    last = nc.tensor.matmul(sq_ps[:, i, :], sq_acc[:, t], fold[:, :], start=True, stop=True)
                last.then_inc(folded, 1)
                pe.wait_ge(x_made, b + 1)
                for i in range(TB):
                    last = nc.tensor.transpose(xh_ps[:, i * P:(i + 1) * P], x[:, i, :], ident[:, :])
                last.then_inc(xT_done, 1)
                pe.wait_ge(xT_copied, b + 1)
                for c in range(HC):
                    nc.tensor.matmul(h1_ps[c][:, :], w1_sb[:, c * P:(c + 1) * P], xT[:, :],
                                     start=True, stop=True).then_inc(h1_done, 1)
                for c in range(HC):
                    pe.wait_ge(h1_made, b * HC + (c + 1))
                    last = nc.tensor.matmul(xh_ps[:, :], w2_sb[:, c, :], h1[:, c, :],
                                            start=(c == 0), stop=(c == HC - 1))
                last.then_inc(h2_done, 1)
                pe.wait_ge(h2_made, b + 1)
                for i in range(TB):
                    t = slice(i * P, (i + 1) * P)
                    nc.tensor.matmul(y_ps[:, i:i + 1], xT[:, t], wl_sb[:, :], start=True, stop=False)
                    last = nc.tensor.matmul(y_ps[:, i:i + 1], h2[:, t], fw_sb[:, :], start=False, stop=True)
                last.then_inc(y_done, 1)

            pe.wait_ge(consts_made, 1)
            turn_where(0, 0)
            pe.wait_ge(part2_made, 2)
            look_up(0, 0)
            pe.wait_ge(ident_made, 2)
            pe.wait_ge(weights_in, 16 * 5)
            pe.wait_ge(consts_made, 6)
            pe.wait_ge(part2_made, MMF)

            with pe.Fori(0, BLOCKS - 1) as b:
                for n in range(1, MMF):
                    look_up(b, n)
                look_up(b + 1, 0)
                mlp(b)
            for n in range(1, MMF):
                look_up(BLOCKS - 1, n, last_field=(n == MMF - 1))
            mlp(BLOCKS - 1)


def kernel(r_ds_input, r_sp_input, L0_rec_emb_tables, L0_rec_lin_tables, L0_rec_lin_w, L0_rec_lin_b,
           L0_rec_w1, L0_rec_b1, L0_rec_w2, L0_rec_b2, L0_rec_fw, L0_rec_fb):
    import numpy as np
    import concourse.bacc as bacc
    from concourse.bass_utils import run_bass_kernel_spmd

    ds, sp, emb, lin, lin_w, lin_b, w1, b1, w2, b2, fw, fb = (np.asarray(a) for a in (
        r_ds_input, r_sp_input, L0_rec_emb_tables, L0_rec_lin_tables, L0_rec_lin_w, L0_rec_lin_b,
        L0_rec_w1, L0_rec_b1, L0_rec_w2, L0_rec_b2, L0_rec_fw, L0_rec_fb))
    B = sp.shape[0]
    F, C, E = emb.shape
    H1, H2 = w1.shape[0], w2.shape[0]
    P, M = 128, 4
    HIS = -(-C // (4 * P)) * 4
    zero = np.zeros((1, H1), w1.dtype)
    one = np.ones((1, 1), w1.dtype)

    def by_lo(a):
        a = np.concatenate([a, np.zeros((M, HIS * P - C, a.shape[2]), a.dtype)], axis=1)
        return a.reshape(M, HIS, P, a.shape[2]).transpose(0, 2, 1, 3).reshape(M, P, HIS * a.shape[2])

    arrays = {
        "dense": ds,
        "sparse": sp,
        "cols": np.ascontiguousarray(sp[:, :M].reshape(P, B // P, M).transpose(2, 1, 0)).reshape(M * (B // P), P),
        "table": np.concatenate([emb, lin], axis=2).reshape(F * C, E + 1),
        "tabs": np.concatenate([by_lo(emb[:M]), by_lo(lin[:M])], axis=2),
        "w1x": np.concatenate([w1.T[:E], zero, w1.T[E:], b1.reshape(1, H1), zero], axis=0),
        "w2t": np.ascontiguousarray(w2.T),
        "b2c": b2.reshape(H2, 1),
        "fwc": fw.reshape(H2, 1),
        "wlx": np.concatenate([zero.reshape(H1, 1)[:E], one, lin_w.T, lin_b.reshape(1, 1), fb.reshape(1, 1)], axis=0),
    }
    nc = bacc.Bacc("TRN2", target_bir_lowering=False, num_devices=1)
    aps = [nc.dram_tensor(n, a.shape, mybir.dt.from_np(a.dtype), kind="ExternalInput").ap()
           for n, a in arrays.items()]
    out = nc.dram_tensor("out", (ds.shape[0], 1), mybir.dt.float32, kind="ExternalOutput").ap()
    build_deep_fm(nc, *aps, out)
    return run_bass_kernel_spmd(nc, [arrays], core_ids=[0]).results[0]["out"]
```

```python
import concourse.bass as bass
from concourse import mybir
from contextlib import ExitStack


def build_deep_fm(nc, dense, sparse, cols, table, tabs, w1x, w2t, b2c, fwc, wlx, out):
    fp32 = mybir.dt.float32
    bf16 = mybir.dt.bfloat16
    f32r = mybir.dt.float32r
    i32 = mybir.dt.int32
    ALU = mybir.AluOpType
    ACT = mybir.ActivationFunctionType
    AX = mybir.AxisListType

    P = 128
    B, DS = dense.shape
    F = sparse.shape[1]
    CATS = table.shape[0] // F
    W = table.shape[1]
    E = W - 1
    H1 = w1x.shape[1]
    H2 = w2t.shape[1]
    HC = H1 // P
    TILES = B // P
    X = w1x.shape[0]
    MMF = tabs.shape[0]
    TW = tabs.shape[2]
    J = P // E
    HIS = TW // W
    CHUNKS = HIS // J
    TB = 4
    BLOCKS = TILES // TB
    N = TB * P
    RING = 5
    SHARED = (4, 0, 1)
    FROM = [MMF if k in SHARED else MMF - 1 for k in range(RING)]
    GF = [F - f for f in FROM]
    GMAX = max(GF)
    PAIRS = MMF // 2
    SJ = 2 * BLOCKS
    LO_BITS = 7
    J_BITS = 2
    GROUPS = 5
    ACT_G = GROUPS - 1
    ACT_GATES = 8
    FIRST = [g * (CHUNKS - ACT_GATES) // ACT_G for g in range(GROUPS)] + [CHUNKS]
    SUB, HI = range(2)
    assert J == 1 << J_BITS and P == 1 << LO_BITS
    assert MMF % 2 == 0 and TILES == PAIRS * RING + 1
    END = 4
    TILE_AT = {1: 0, 3: 1, 4: 2, 6: 3, 7: 4}
    PIECE = [slice(FIRST[g] * P, FIRST[g + 1] * P if g < GROUPS - 1 else TW) for g in range(GROUPS)]
    PIECES_AT = [[0, 1], [2], [3], [4]]
    ORDER = [(k, b) for k in range(2) for b in range(BLOCKS)]
    LAST_ORDER = [(0, 0), (0, 1), (1, 0), (1, 1), (0, 2), (1, 2), (0, 3), (1, 3)]
    LAST_JOB = [max(i for i, (k, b) in enumerate(LAST_ORDER) if b == m) for m in range(BLOCKS)]
    LAST_TILE_AT = {1: 0, 3: 1, 4: 2, 6: 3}
    LAST_PIECES_AT = [[0, 1, 2], [3, 4]]
    MLP_A = {3: 0, 5: 1, 7: 2}
    MLP_B = {4: 0, 6: 1}
    assert BLOCKS == 4

    def columns(k, b):
        if k == 0:
            return slice(0, N)
        mine = [t for t in range(TB) if (b * TB + t) % RING in SHARED]
        assert mine == list(range(mine[0], mine[-1] + 1))
        return slice(mine[0] * P, (mine[-1] + 1) * P)

    LAST_COLS = [columns(k, b) for k, b in LAST_ORDER]
    COLS = [slice(0, N)] * SJ

    codes_dram = nc.dram_tensor("codes_dram", (2, MMF * TILES, P), bf16).ap()

    ctx = ExitStack()
    with ctx:
        def sb(name, shape, dt=fp32):
            return ctx.enter_context(nc.sbuf_tensor(name, shape, dt))

        def pb(name, shape, dt=fp32):
            return ctx.enter_context(nc.psum_tensor(name, shape, dt))

        def sem(name):
            return ctx.enter_context(nc.semaphore(name))

        field_base = sb("field_base", [P, F], i32)
        row_idx = sb("row_idx", [P, TILES * F], i32)
        idx_now = [sb(f"idx_now{k}", [P, GMAX], i32) for k in range(RING)]
        rows = [sb(f"rows{k}", [P, GMAX * W]) for k in range(RING)]
        squares = sb("squares", [P, GMAX * E])
        g_sum = sb("g_sum", [P, TILES, W])
        g_sq = sb("g_sq", [P, TILES, E])
        CR = MMF * TILES
        col_raw = sb("col_raw", [CR, P], i32)
        col_wrap = sb("col_wrap", [CR, P], i32)
        col_clip = sb("col_clip", [CR, P], i32)
        col_bits = sb("col_bits", [CR, 2, P], i32)
        col_code = sb("col_code", [CR, 2, P], bf16)
        codes = [sb(f"codes{k}", [P, 2, N], bf16) for k in range(2)]
        mm_clip = sb("mm_clip", [P, MMF, TILES], i32)
        lo_i = sb("lo_i", [P, MMF * TILES], i32)
        chunk_i = sb("chunk_i", [P, MMF * TILES], i32)
        lo_of = sb("lo_of", [P, MMF * TILES])
        chunk_of = sb("chunk_of", [P, MMF * TILES])
        column_i = sb("column_i", [P, P], i32)
        column = sb("column", [P, P], bf16)
        ident_bf = sb("ident_bf", [P, P], bf16)
        whereT = [sb(f"whereT{k}", [P, N], bf16) for k in range(2)]
        where_sb = [sb(f"where_sb{k}", [P, N], bf16) for k in range(2)]
        part_i = sb("part_i", [P, 1], i32)
        sub_i = sb("sub_i", [P, 1], i32)
        part_id = sb("part_id", [P, 1])
        sub_id = sb("sub_id", [P, 1])
        stage = [sb(f"stage{k}", [P, TW]) for k in range(2)]
        high = [sb(f"high{k}", [P, TW], f32r) for k in range(2)]
        low = [sb(f"low{k}", [P, TW], f32r) for k in range(2)]
        gates = sb("gates", [P, CHUNKS + 1, N], f32r)
        distance = sb("distance", [P, ACT_GATES, N], bf16)
        minus_chunk_i = sb("minus_chunk_i", [P, ACT_GATES], i32)
        minus_chunk = sb("minus_chunk", [P, ACT_GATES])
        picked_emb = sb("picked_emb", [P, N])
        picked_lin = sb("picked_lin", [HIS, N])
        picked_sq = sb("picked_sq", [P, N])
        emb_acc = sb("emb_acc", [P, BLOCKS * N])
        idx_raw = emb_acc[:, 0:TILES * F].bitcast(i32)
        idx_wrap = emb_acc[:, TILES * F:2 * TILES * F].bitcast(i32)
        lin_acc = sb("lin_acc", [P, BLOCKS * N])
        sq_acc = sb("sq_acc", [P, BLOCKS * N])
        dense_sb = sb("dense_sb", [P, TILES * DS])
        h1 = stage[0][:, 0:HC * N].rearrange("p (c n) -> p c n", n=N)
        h2 = stage[0][:, HC * N:(HC + 1) * N]
        xT = [stage[m >= BLOCKS - 1][0:X, (HC + 1) * N:(HC + 2) * N] for m in range(BLOCKS + 1)]
        SUMS = (HC + 2) * N
        sum_all = stage[0][:, SUMS:SUMS + TB * W].rearrange("p (i w) -> p i w", w=W)
        sq_all = stage[0][:, SUMS + TB * W:SUMS + TB * (W + E)].rearrange("p (i e) -> p i e", e=E)
        half_sq = stage[0][:, SUMS + TB * (W + E):SUMS + TB * (W + 2 * E)].rearrange("p (i e) -> p i e", e=E)
        XS = SUMS + TB * (W + 2 * E)
        x = stage[0][:, XS:XS + TB * P].rearrange("p (i x) -> p i x", x=P)
        y = sb("y", [P, TILES])
        ident = sb("ident", [P, P])
        fold = sb("fold", [P, E])
        ones = sb("ones", [P, 1])
        w1_sb = sb("w1_sb", [X, H1])
        w2_sb = sb("w2_sb", [P, HC, H2])
        b2_sb = sb("b2_sb", [H2, 1])
        fw_sb = sb("fw_sb", [H2, 1])
        wl_sb = sb("wl_sb", [X, 1])

        small_ps = pb("small_ps", [P, N])
        xh_ps = pb("xh_ps", [P, N])
        h1_ps = [pb("h1_ps0", [P, N]), small_ps]
        lin_cand = pb("lin_cand", [P, N])
        cand = [pb(f"cand{k}", [P, N]) for k in range(2)]
        where = [pb(f"where{k}", [P, 2 * N], bf16) for k in range(2)]
        fold_at = [small_ps] * (BLOCKS - 1) + [cand[0]]
        sum_ps = [at[:, 0:TB * W].rearrange("p (i w) -> p i w", w=W) for at in fold_at]
        sq_ps = [at[:, TB * W:TB * (W + E)].rearrange("p (i e) -> p i e", e=E) for at in fold_at]
        xT_ps = [xh_ps] * (BLOCKS - 1) + [lin_cand] * 2
        y_ps = small_ps[:, TB * (W + E):TB * (W + E + 1)]

        idx_in = sem("idx_in")
        cols_in = sem("cols_in")
        dense_in = sem("dense_in")
        weights_in = sem("weights_in")
        stage_in = [sem(f"stage_in{k}") for k in range(2)]
        first_in = [sem(f"first_in{g}") for g in range(GROUPS)]
        codes_out = sem("codes_out")
        codes_in = [sem(f"codes_in{k}") for k in range(2)]
        base_made = sem("base_made")
        ident_made = sem("ident_made")
        idx_step = sem("idx_step")
        col_step = sem("col_step")
        id_step = sem("id_step")
        idx_set = sem("idx_set")
        consts_made = sem("consts_made")
        high_made = sem("high_made")
        low_made = sem("low_made")
        distance_made = sem("distance_made")
        act_gates_made = sem("act_gates_made")
        gathered = [sem(f"gathered{k}") for k in range(RING)]
        gathered_end = sem("gathered_end")
        squared = sem("squared")
        reduced = sem("reduced")
        mm_step = sem("mm_step")
        whereT_made = sem("whereT_made")
        where_made = sem("where_made")
        where_copied = sem("where_copied")
        gates_made = sem("gates_made")
        gates_free = sem("gates_free")
        emb_picked = sem("emb_picked")
        cand_free = sem("cand_free")
        picked_squared = sem("picked_squared")
        summed = sem("summed")
        folded = sem("folded")
        totals = sem("totals")
        half_made = sem("half_made")
        x_ones = sem("x_ones")
        x_made = sem("x_made")
        xT_done = sem("xT_done")
        xT_copied = sem("xT_copied")
        h1_done = sem("h1_done")
        h1_made = sem("h1_made")
        h2_done = sem("h2_done")
        h2_made = sem("h2_made")
        y_done = sem("y_done")
        y_made = sem("y_made")
        stored = sem("stored")

        block = ctx.enter_context(nc.Block())

        @block.sync
        def _(sp):
            def load_table(n, k):
                sp.dma_start(stage[k][:, :], tabs[bass.ds(n, 1), :, :].rearrange("o p c -> (o p) c")
                             ).then_inc(stage_in[k], 16)

            sp.dma_start(idx_raw[:, :], sparse.rearrange("(p t) f -> p (t f)", p=P)).then_inc(idx_in, 16)
            for g in range(GROUPS):
                sp.dma_start(stage[0][:, PIECE[g]], tabs[0, :, PIECE[g]]).then_inc(first_in[g], 16)
            sp.dma_start(col_raw[:, :], cols).then_inc(cols_in, 16)
            sp.dma_start(dense_sb[:, :], dense.rearrange("(p t) d -> p (t d)", p=P)).then_inc(dense_in, 16)
            load_table(1, 1)
            sp.wait_ge(col_step, 8)
            sp.dma_start(codes_dram.rearrange("q r p -> r q p"), col_code[:, :, :]).then_inc(codes_out, 16)
            sp.wait_ge(codes_out, 16)

            def load_codes(p, i, order=ORDER):
                sp.wait_ge(cand_free, p * SJ + (i + 1))
                k, b = order[i]
                src = codes_dram[:, bass.ds(p * (SJ * TB) + (k * BLOCKS + b) * TB, TB), :].rearrange("q t p -> q (t p)")
                sp.dma_start(codes[i % 2][:, :, :], src.unsqueeze(0).broadcast_to([P, 2, N])).then_inc(codes_in[i % 2], 16)

            def weights():
                sp.dma_start(w1_sb[:, :], w1x).then_inc(weights_in, 16)
                sp.dma_start(w2_sb[:, :, :], w2t.rearrange("(c p) n -> p c n", p=P)).then_inc(weights_in, 16)
                sp.dma_start(b2_sb[:, :], b2c).then_inc(weights_in, 16)
                sp.dma_start(fw_sb[:, :], fwc).then_inc(weights_in, 16)
                sp.dma_start(wl_sb[:, :], wlx).then_inc(weights_in, 16)

            with sp.Fori(0, PAIRS - 1) as p:
                for i in range(SJ):
                    if i % BLOCKS == 0:
                        sp.wait_ge(low_made, (p * 2 + (i // BLOCKS + 1)) * GROUPS)
                        load_table(p * 2 + (i // BLOCKS + 2), i // BLOCKS)
                    load_codes(p, i)
            weights()
            for i in range(len(LAST_ORDER)):
                load_codes(PAIRS - 1, i, LAST_ORDER)
            sp.wait_ge(y_made, BLOCKS + 1)
            sp.dma_start(out.rearrange("(p t) o -> p (t o)", p=P), y[:, :]).then_inc(stored, 16)
            sp.wait_ge(stored, 16)

        @block.gpsimd
        def _(pool):
            pool.iota(field_base[:, :], pattern=[[CATS, F]], base=0,
                      channel_multiplier=0).then_inc(base_made, 1)
            pool.iota(part_i[:, :], pattern=[[0, 1]], base=0, channel_multiplier=1).then_inc(base_made, 1)
            pool.iota(column_i[:, :], pattern=[[1, P]], base=0, channel_multiplier=0).then_inc(base_made, 1)
            pool.iota(minus_chunk_i[:, :], pattern=[[-1, ACT_GATES]], base=-(FIRST[ACT_G] + 1),
                      channel_multiplier=0).then_inc(base_made, 1)
            pool.memset(ident[:, :], 0.0).then_inc(ident_made, 1)
            pool.wait_ge(ident_made, 1)
            pool.affine_select(out=ident[:, :], in_=ident[:, :], compare_op=ALU.not_equal, fill=1.0,
                               base=0, pattern=[[-1, P]], channel_multiplier=1).then_inc(ident_made, 1)
            pool.memset(lin_acc[:, :], 0.0).then_inc(summed, 1)

            def gather(k, f, done):
                pool.indirect_dma_start(
                    out=rows[k][:, f * W:(f + 1) * W], out_offset=None,
                    in_=table[:, :],
                    in_offset=bass.IndirectOffsetOnAxis(ap=idx_now[k][:, f:f + 1], axis=0),
                ).then_inc(done, 16)

            with pool.Fori(0, PAIRS) as p:
                for k in range(RING):
                    pool.wait_ge(idx_set, p * RING + (k + 1))
                    pool.nop(nofuse=True)
                    for f in range(GF[k]):
                        gather(k, f, gathered[k])
            pool.wait_ge(idx_set, TILES)
            for f in range(GF[0]):
                gather(0, f, gathered[0] if f < GF[0] - END else gathered_end)

        @block.vector
        def _(dve):
            dve.wait_ge(base_made, 4)
            dve.wait_ge(ident_made, 2)
            nc.vector.tensor_copy(ident_bf[:, :], ident[:, :]).then_inc(consts_made, 1)
            nc.vector.tensor_copy(column[:, :], column_i[:, :]).then_inc(mm_step, 1)
            nc.vector.tensor_scalar(sub_i[:, :], part_i[:, :], E.bit_length() - 1, None,
                                    ALU.arith_shift_right).then_inc(id_step, 1)
            nc.vector.tensor_copy(part_id[:, :], part_i[:, :]).then_inc(consts_made, 1)
            dve.wait_ge(id_step, 1)
            nc.vector.tensor_copy(sub_id[:, :], sub_i[:, :]).then_inc(consts_made, 1)
            nc.vector.tensor_reduce(fold[:, :], ident[:, :].rearrange("p (j e) -> p e j", j=J), AX.X,
                                    ALU.add).then_inc(consts_made, 1)
            nc.vector.tensor_copy(minus_chunk[:, :], minus_chunk_i[:, :]).then_inc(consts_made, 1)
            nc.vector.memset(ones[:, :], 1.0).then_inc(consts_made, 1)
            nc.vector.memset(picked_sq[:, 0:1], 0.0).then_inc(cand_free, 2)
            nc.vector.memset(picked_sq[:, 1:2], 0.0).then_inc(gates_free, GROUPS)

            dve.wait_ge(idx_in, 16)

            def table_rows(step, t0, t1):
                c = slice(t0 * F, t1 * F)
                nc.vector.tensor_scalar(idx_raw[:, c], idx_raw[:, c], CATS - 1, None, ALU.min).then_inc(idx_step, 1)
                dve.wait_ge(idx_step, step + 1)
                nc.vector.tensor_scalar(idx_wrap[:, c], idx_raw[:, c], 0, CATS, ALU.is_lt,
                                        ALU.mult).then_inc(idx_step, 1)
                dve.wait_ge(idx_step, step + 2)
                nc.vector.tensor_tensor(idx_wrap[:, c], idx_raw[:, c], idx_wrap[:, c], ALU.add).then_inc(idx_step, 1)
                dve.wait_ge(idx_step, step + 3)
                nc.vector.scalar_tensor_tensor(
                    row_idx[:, c].rearrange("p (t f) -> p t f", f=F), idx_wrap[:, c].rearrange("p (t f) -> p t f", f=F),
                    0, field_base[:, :].unsqueeze(1).broadcast_to([P, t1 - t0, F]), ALU.max, ALU.add).then_inc(idx_step, 1)

            table_rows(0, 0, RING)
            dve.wait_ge(idx_step, 4)
            for k in range(RING):
                nc.vector.tensor_copy(idx_now[k][:, 0:GF[k]], row_idx[:, k * F + FROM[k]:(k + 1) * F]).then_inc(idx_set, 1)
            table_rows(4, RING, TILES)
            dve.wait_ge(idx_step, 8)

            def low_part(g, number, k):
                dve.wait_ge(high_made, number)
                nc.vector.tensor_tensor(low[k][:, PIECE[g]], stage[k][:, PIECE[g]], high[k][:, PIECE[g]],
                                        ALU.subtract).then_inc(low_made, 1)

            def make_whereT(p, i, order=ORDER, cols=COLS):
                k, b = order[i]
                for t in range(cols[i].start // P, cols[i].stop // P):
                    at = bass.ds(p * (SJ * TB) + ((k * BLOCKS + b) * TB + t), 1)
                    last = nc.vector.tensor_scalar(whereT[i % 2][:, t * P:(t + 1) * P], column[:, :],
                                                   lo_of[:, at], chunk_of[:, at], ALU.is_equal, ALU.mult)
                last.then_inc(whereT_made, 1)

            def make_gates(p, i, g0, g1, cols=COLS):
                j = p * SJ + i
                w = where_sb[i % 2][:, cols[i]]
                dve.wait_ge(where_copied, j + 1)
                for g in range(g0, g1):
                    dve.wait_ge(gates_free, j * GROUPS + (g + 1))
                    if g == ACT_G:
                        last = nc.vector.tensor_scalar(gates[:, CHUNKS, cols[i]], w, 0.0, None, ALU.is_gt)
                    else:
                        for c in range(FIRST[g], FIRST[g + 1]):
                            last = nc.vector.tensor_scalar(gates[:, c, cols[i]], w, float(c + 1), None, ALU.is_equal)
                    last.then_inc(gates_made, 1)

            def pick(p, i, b, w):
                j = p * SJ + i
                c = slice(b * N + w.start, b * N + w.stop)
                dve.wait_ge(gates_free, (j + 2) * GROUPS)
                dve.wait_ge(codes_in[i % 2], p * (16 * SJ // 2) + 16 * (i // 2 + 1))
                dve.wait_ge(summed, (j + 1) * 3)
                nc.vector.scalar_tensor_tensor(picked_emb[:, w], codes[i % 2][:, SUB, w], sub_id[:, 0:1],
                                               cand[i % 2][:, w], ALU.is_equal, ALU.mult).then_inc(emb_picked, 1)
                nc.vector.scalar_tensor_tensor(picked_lin[:, w], codes[i % 2][0:HIS, HI, w], part_id[0:HIS, 0:1],
                                               lin_cand[0:HIS, w], ALU.is_equal, ALU.mult).then_inc(cand_free, 1)
                dve.wait_ge(emb_picked, j + 1)
                nc.vector.tensor_tensor(emb_acc[:, c], emb_acc[:, c], picked_emb[:, w], ALU.add).then_inc(summed, 1)
                dve.wait_ge(cand_free, j + 3)
                nc.vector.tensor_tensor(lin_acc[0:HIS, c], lin_acc[0:HIS, c], picked_lin[:, w], ALU.add).then_inc(summed, 1)

            def add_squares(p, i, b, w):
                c = slice(b * N + w.start, b * N + w.stop)
                dve.wait_ge(picked_squared, p * SJ + (i + 1))
                nc.vector.tensor_tensor(sq_acc[:, c], sq_acc[:, c], picked_sq[:, w], ALU.add).then_inc(summed, 1)

            def sum_tile(p, k, set_next=True):
                t, g = p * RING + k, GF[k]
                dve.wait_ge(gathered[k], (p + 1) * (16 * GF[k]))
                nc.vector.tensor_reduce(
                    g_sum[:, bass.ds(t, 1), :].rearrange("p o w -> p (o w)"),
                    rows[k][:, 0:g * W].rearrange("p (f w) -> p w f", w=W), AX.X, ALU.add).then_inc(reduced, 1)
                dve.wait_ge(squared, t + 1)
                nc.vector.tensor_reduce(
                    g_sq[:, bass.ds(t, 1), :].rearrange("p o e -> p (o e)"),
                    squares[:, 0:g * E].rearrange("p (f e) -> p e f", e=E), AX.X, ALU.add).then_inc(reduced, 1)
                if set_next:
                    dve.wait_ge(reduced, t * 2 + 2)
                    nc.vector.tensor_copy(idx_now[k][:, 0:g],
                                          row_idx[:, bass.ds((t + RING) * F + FROM[k], g)]).then_inc(idx_set, 1)

            def add_parts(m, k1):
                dve.wait_ge(folded, m + 1)
                dve.wait_ge(reduced, 2 * (m * TB + k1))
                t = slice(m * TB, m * TB + k1)
                nc.vector.tensor_tensor(sum_all[:, 0:k1, :], g_sum[:, t, :], sum_ps[m][:, 0:k1, :],
                                        ALU.add).then_inc(totals, 1)
                nc.vector.tensor_tensor(sq_all[:, 0:k1, :], g_sq[:, t, :], sq_ps[m][:, 0:k1, :],
                                        ALU.add).then_inc(totals, 1)
                if k1 < TB:
                    nc.vector.tensor_copy(sum_all[:, k1:TB, :], sum_ps[m][:, k1:TB, :]).then_inc(totals, 1)
                    nc.vector.tensor_copy(sq_all[:, k1:TB, :], sq_ps[m][:, k1:TB, :]).then_inc(totals, 1)
                dve.wait_ge(totals, 2 * m + (2 if k1 == TB else 4))

            def copy_dense(b):
                dve.wait_ge(x_ones, 1)
                nc.vector.tensor_copy(x[:, :, W:W + DS], dense_sb[:, b * (TB * DS):(b + 1) * (TB * DS)]
                                      .rearrange("p (i d) -> p i d", d=DS))

            def make_x(m, k0, k1):
                nc.vector.scalar_tensor_tensor(half_sq[:, k0:k1, :], sum_all[:, k0:k1, 0:E], 0.5,
                                               sum_all[:, k0:k1, 0:E], ALU.mult, ALU.mult).then_inc(half_made, 1)
                nc.vector.tensor_copy(x[:, k0:k1, E:W], sum_all[:, k0:k1, E:W])
                dve.wait_ge(half_made, m + 1)
                nc.vector.scalar_tensor_tensor(x[:, k0:k1, 0:E], sq_all[:, k0:k1, :], -0.5, half_sq[:, k0:k1, :],
                                               ALU.mult, ALU.add).then_inc(x_made, 1)

            def copy_xT(m, k0, k1):
                dve.wait_ge(xT_done, m + 1)
                nc.vector.tensor_copy(xT[m][:, k0 * P:k1 * P], xT_ps[m][0:X, k0 * P:k1 * P]).then_inc(xT_copied, 1)

            nc.vector.tensor_scalar(mm_clip[:, :, :], idx_wrap[:, :].rearrange("p (t f) -> p f t", f=F)[:, 0:MMF, :],
                                    0, None, ALU.max).then_inc(mm_step, 1)
            dve.wait_ge(mm_step, 2)
            mm_flat = mm_clip[:, :, :].rearrange("p n t -> p (n t)")
            nc.vector.tensor_scalar(lo_i[:, :], mm_flat, P - 1, None, ALU.bitwise_and).then_inc(mm_step, 1)
            nc.vector.tensor_scalar(chunk_i[:, :], mm_flat, LO_BITS + J_BITS, None,
                                    ALU.arith_shift_right).then_inc(mm_step, 1)
            dve.wait_ge(mm_step, 4)
            nc.vector.tensor_copy(lo_of[:, :], lo_i[:, :]).then_inc(mm_step, 1)
            nc.vector.tensor_scalar(chunk_of[:, :], chunk_i[:, :], 1, None, ALU.add).then_inc(mm_step, 1)
            dve.wait_ge(mm_step, 6)
            make_whereT(0, 0)
            for g in range(GROUPS):
                low_part(g, g + 1, 0)
                make_gates(0, 0, g, g + 1)
                if g == 0:
                    make_whereT(0, 1)

            dve.wait_ge(cols_in, 16)
            nc.vector.tensor_scalar(col_raw[:, :], col_raw[:, :], CATS - 1, None, ALU.min).then_inc(col_step, 1)
            dve.wait_ge(col_step, 1)
            nc.vector.tensor_scalar(col_wrap[:, :], col_raw[:, :], 0, CATS, ALU.is_lt, ALU.mult).then_inc(col_step, 1)
            dve.wait_ge(col_step, 2)
            nc.vector.tensor_tensor(col_wrap[:, :], col_raw[:, :], col_wrap[:, :], ALU.add).then_inc(col_step, 1)
            dve.wait_ge(col_step, 3)
            nc.vector.tensor_scalar(col_clip[:, :], col_wrap[:, :], 0, None, ALU.max).then_inc(col_step, 1)
            dve.wait_ge(col_step, 4)
            nc.vector.tensor_scalar(col_bits[:, SUB, :], col_clip[:, :], LO_BITS, J - 1,
                                    ALU.arith_shift_right, ALU.bitwise_and).then_inc(col_step, 1)
            nc.vector.tensor_scalar(col_bits[:, HI, :], col_clip[:, :], LO_BITS, None,
                                    ALU.arith_shift_right).then_inc(col_step, 1)
            dve.wait_ge(col_step, 6)
            for q in (SUB, HI):
                nc.vector.tensor_copy(col_code[:, q, :], col_bits[:, q, :]).then_inc(col_step, 1)

            dve.wait_ge(dense_in, 16)

            def body(p, last=False):
                order, pieces = (LAST_ORDER, LAST_PIECES_AT) if last else (ORDER, PIECES_AT * 2)
                tile_at, cols = (LAST_TILE_AT, LAST_COLS) if last else (TILE_AT, COLS)
                for i, (k, b) in enumerate(order):
                    ahead = not (last and i == len(order) - 1)
                    if not (last and i >= len(order) - 2):
                        make_whereT(p + (i + 2) // SJ, (i + 2) % SJ, order, cols)
                    if ahead:
                        make_gates(p + (i + 1) // SJ, (i + 1) % SJ, 0, 2, cols)
                    if i < len(pieces):
                        for g in pieces[i]:
                            low_part(g, (p * 2 + (k + 1)) * GROUPS + (g + 1), (k + 1) % 2)
                    if last and i == 2:
                        nc.vector.memset(x[:, :, :], 1.0).then_inc(x_ones, 1)
                    if ahead:
                        make_gates(p + (i + 1) // SJ, (i + 1) % SJ, 2, 3, cols)
                    if last and i in MLP_A:
                        m = MLP_A[i]
                        add_parts(m, TB)
                        copy_dense(m)
                        make_x(m, 0, TB)
                    if ahead:
                        make_gates(p + (i + 1) // SJ, (i + 1) % SJ, 3, GROUPS, cols)
                    pick(p, i, b, cols[i])
                    if last and i in MLP_A:
                        copy_xT(MLP_A[i], 0, TB)
                    if i in tile_at:
                        sum_tile(p, tile_at[i], not last or tile_at[i] == 0)
                    add_squares(p, i, b, cols[i])

            with dve.Fori(0, PAIRS - 1) as p:
                body(p)
            body(PAIRS - 1, last=True)
            m, k, t, split = BLOCKS - 1, TB - 1, TILES - 1, GF[0] - END
            sum_tile(PAIRS - 1, RING - 1, False)
            add_parts(m, k)
            copy_dense(m)
            make_x(m, 0, k)
            copy_xT(m, 0, k)

            for h, (f0, f1) in enumerate(((0, split), (split, GF[0]))):
                if h == 0:
                    dve.wait_ge(gathered[0], PAIRS * (16 * GF[0]) + 16 * split)
                else:
                    dve.wait_ge(gathered_end, 16 * END)
                nc.vector.tensor_reduce(g_sum[:, t, :], rows[0][:, f0 * W:f1 * W].rearrange("p (f w) -> p w f", w=W),
                                        AX.X, ALU.add).then_inc(reduced, 1)
                dve.wait_ge(reduced, 2 * t + 2 * h + 1)
                nc.vector.tensor_tensor(sum_all[:, k, :], sum_all[:, k, :], g_sum[:, t, :], ALU.add).then_inc(totals, 1)
                dve.wait_ge(squared, TILES + h)
                nc.vector.tensor_reduce(g_sq[:, t, :], squares[:, f0 * E:f1 * E]
                                        .rearrange("p (f e) -> p e f", e=E), AX.X, ALU.add).then_inc(reduced, 1)
                dve.wait_ge(reduced, 2 * t + 2 * h + 2)
                nc.vector.tensor_tensor(sq_all[:, k, :], sq_all[:, k, :], g_sq[:, t, :], ALU.add).then_inc(totals, 1)
                dve.wait_ge(totals, 2 * BLOCKS + 2 + 2 * (h + 1))
            make_x(BLOCKS, k, TB)
            copy_xT(BLOCKS, k, TB)

        @block.scalar
        def _(act):
            def high_part(g, k):
                nc.scalar.copy(high[k][:, PIECE[g]], stage[k][:, PIECE[g]]).then_inc(high_made, 1)

            def copy_where(p, i, cols=COLS):
                act.wait_ge(where_made, p * SJ + (i + 1))
                nc.scalar.copy(where_sb[i % 2][:, cols[i]], where[i % 2][:, cols[i]]).then_inc(where_copied, 1)

            def measure(p, i, cols=COLS):
                act.wait_ge(where_copied, p * SJ + (i + 1))
                for c in range(ACT_GATES):
                    last = nc.scalar.activation(distance[:, c, cols[i]], where_sb[i % 2][:, cols[i]], ACT.Square,
                                                bias=minus_chunk[:, c:c + 1])
                last.then_inc(distance_made, 1)

            def make_gates(p, i, cols=COLS):
                act.wait_ge(gates_free, (p * SJ + (i + 1)) * GROUPS)
                act.wait_ge(distance_made, p * SJ + (i + 1))
                nc.scalar.activation(gates[:, FIRST[ACT_G]:CHUNKS, cols[i]], distance[:, :, cols[i]], ACT.Relu,
                                     bias=ones[:, 0:1], scale=-1.0).then_inc(act_gates_made, 1)

            def square_picked(p, i, w):
                act.wait_ge(emb_picked, p * SJ + (i + 1))
                nc.scalar.activation(picked_sq[:, w], picked_emb[:, w], ACT.Square).then_inc(picked_squared, 1)

            def square_rows(k, f0, f1):
                nc.scalar.activation(
                    squares[:, f0 * E:f1 * E].rearrange("p (f e) -> p f e", e=E),
                    rows[k][:, f0 * W:f1 * W].rearrange("p (f w) -> p f w", w=W)[:, :, 0:E],
                    ACT.Square).then_inc(squared, 1)

            def relus(m, k0, k1):
                t = slice(k0 * P, k1 * P)
                for c in range(HC):
                    act.wait_ge(h1_done, m * HC + (c + 1))
                    nc.scalar.activation(h1[:, c, t], h1_ps[c][:, t], ACT.Relu).then_inc(h1_made, 1)
                act.wait_ge(h2_done, m + 1)
                nc.scalar.activation(h2[:, t], xh_ps[:, t], ACT.Relu, bias=b2_sb[:, 0:1]).then_inc(h2_made, 1)

            def sigmoid(b, m, k0, k1):
                act.wait_ge(y_done, m + 1)
                nc.scalar.activation(y[:, b * TB + k0:b * TB + k1], y_ps[:, k0:k1], ACT.Sigmoid).then_inc(y_made, 1)

            act.wait_ge(summed, 1)
            nc.scalar.copy(sq_acc[:, :], lin_acc[:, :]).then_inc(summed, 1)
            for g in range(GROUPS):
                act.wait_ge(first_in[g], 16)
                high_part(g, 0)
                if g == 0:
                    copy_where(0, 0)
                if g == 1:
                    act.wait_ge(consts_made, 6)
                    measure(0, 0)
            make_gates(0, 0)
            act.wait_ge(mm_step, 6)
            nc.scalar.copy(emb_acc[:, :], lin_acc[:, :]).then_inc(summed, 1)

            def square_tile(p, k):
                act.wait_ge(gathered[k], (p + 1) * (16 * GF[k]))
                square_rows(k, 0, GF[k])

            def body(p, last=False):
                order, pieces = (LAST_ORDER, LAST_PIECES_AT) if last else (ORDER, PIECES_AT * 2)
                tile_at, cols = (LAST_TILE_AT, LAST_COLS) if last else (TILE_AT, COLS)
                for i, (k, b) in enumerate(order):
                    ahead = not (last and i == len(order) - 1)
                    if ahead:
                        copy_where(p + (i + 1) // SJ, (i + 1) % SJ, cols)
                    if i < len(pieces):
                        if b == 0:
                            act.wait_ge(stage_in[(k + 1) % 2], p * 16 + 16)
                            act.wait_ge(gates_free, (p * SJ + (i + 1)) * GROUPS)
                        for g in pieces[i]:
                            high_part(g, (k + 1) % 2)
                    if ahead:
                        measure(p + (i + 1) // SJ, (i + 1) % SJ, cols)
                    if last and i in MLP_B:
                        relus(MLP_B[i], 0, TB)
                    if ahead:
                        make_gates(p + (i + 1) // SJ, (i + 1) % SJ, cols)
                    if last and i in MLP_B:
                        sigmoid(MLP_B[i], MLP_B[i], 0, TB)
                    square_picked(p, i, cols[i])
                    if i in tile_at:
                        square_tile(p, tile_at[i])

            with act.Fori(0, PAIRS - 1) as p:
                body(p)
            act.wait_ge(weights_in, 16 * 5)
            body(PAIRS - 1, last=True)
            m, k, split = BLOCKS - 1, TB - 1, GF[0] - END
            relus(m - 1, 0, TB)
            sigmoid(m - 1, m - 1, 0, TB)
            act.wait_ge(reduced, 2 * (TILES - 2))
            square_tile(PAIRS - 1, RING - 1)
            relus(m, 0, k)
            act.wait_ge(gathered[0], PAIRS * (16 * GF[0]) + 16 * split)
            act.wait_ge(reduced, 2 * (TILES - 1))
            square_rows(0, 0, split)
            sigmoid(m, m, 0, k)
            act.wait_ge(gathered_end, 16 * END)
            square_rows(0, split, GF[0])
            relus(BLOCKS, k, TB)
            sigmoid(m, BLOCKS, k, TB)

        @block.tensor
        def _(pe):
            def turn_where(p, i, cols=COLS):
                pe.wait_ge(whereT_made, p * SJ + (i + 1))
                for t in range(cols[i].start // P, cols[i].stop // P):
                    last = nc.tensor.transpose(where[i % 2][:, t * P:(t + 1) * P],
                                               whereT[i % 2][:, t * P:(t + 1) * P], ident_bf[:, :])
                last.then_inc(where_made, 1)

            def look_up(p, i, order=ORDER, cols=COLS, ahead=True, between=()):
                j = p * SJ + i
                (k, b), w = order[i], cols[i]
                pe.wait_ge(cand_free, j + 1)
                for g in range(GROUPS):
                    if b == 0:
                        pe.wait_ge(low_made, (p * 2 + k) * GROUPS + (g + 1))
                    if g == ACT_G:
                        pe.wait_ge(act_gates_made, j + 1)
                    else:
                        pe.wait_ge(gates_made, j * GROUPS + (g + 1))
                    for c in range(FIRST[g], FIRST[g + 1]):
                        for s, part in enumerate((high, low)):
                            last = nc.tensor.matmul(cand[i % 2][:, w], part[k][:, c * P:(c + 1) * P],
                                                    gates[:, c, w], start=(c == 0 and s == 0),
                                                    stop=(c == CHUNKS - 1 and s == 1))
                    if g < GROUPS - 1:
                        last.then_inc(gates_free, 1)
                    if g == 0 and ahead:
                        turn_where(p + (i + 1) // SJ, (i + 1) % SJ, cols)
                    if g in between:
                        between[g]()
                pe.wait_ge(cand_free, j + 2)
                pe.wait_ge(gates_made, (j + 1) * GROUPS)
                for s, part in enumerate((high, low)):
                    last = nc.tensor.matmul(lin_cand[0:HIS, w], part[k][:, CHUNKS * P:CHUNKS * P + HIS],
                                            gates[:, CHUNKS, w], start=(s == 0), stop=(s == 1))
                last.then_inc(gates_free, 1)

            def fold_sums(m):
                if 0 < m < BLOCKS - 1:
                    pe.wait_ge(y_made, m)
                pe.wait_ge(summed, 3 * ((PAIRS - 1) * SJ + LAST_JOB[m] + 2))
                for i in range(TB):
                    t = slice((m * TB + i) * P, (m * TB + i + 1) * P)
                    nc.tensor.matmul(sum_ps[m][:, i, 0:E], emb_acc[:, t], fold[:, :], start=True, stop=True)
                    nc.tensor.matmul(sum_ps[m][:, i, E:W], lin_acc[0:HIS, t], ones[0:HIS, :], start=True, stop=True)
                    last = nc.tensor.matmul(sq_ps[m][:, i, :], sq_acc[:, t], fold[:, :], start=True, stop=True)
                last.then_inc(folded, 1)

            def turn_x(m, k0, k1):
                pe.wait_ge(x_made, m + 1)
                for i in range(k0, k1):
                    last = nc.tensor.transpose(xT_ps[m][:, i * P:(i + 1) * P], x[:, i, :], ident[:, :])
                last.then_inc(xT_done, 1)

            def layer1(m, k0, k1):
                pe.wait_ge(xT_copied, m + 1)
                tiles = slice(k0 * P, k1 * P)
                for c in range(HC):
                    nc.tensor.matmul(h1_ps[c][:, tiles], w1_sb[:, c * P:(c + 1) * P], xT[m][:, tiles],
                                     start=True, stop=True).then_inc(h1_done, 1)

            def layer2(m, k0, k1):
                tiles = slice(k0 * P, k1 * P)
                for c in range(HC):
                    pe.wait_ge(h1_made, m * HC + (c + 1))
                    last = nc.tensor.matmul(xh_ps[:, tiles], w2_sb[:, c, :], h1[:, c, tiles],
                                            start=(c == 0), stop=(c == HC - 1))
                last.then_inc(h2_done, 1)

            def layer3(m, k0, k1):
                pe.wait_ge(h2_made, m + 1)
                for i in range(k0, k1):
                    t = slice(i * P, (i + 1) * P)
                    nc.tensor.matmul(y_ps[:, i:i + 1], xT[m][:, t], wl_sb[:, :], start=True, stop=False)
                    last = nc.tensor.matmul(y_ps[:, i:i + 1], h2[:, t], fw_sb[:, :], start=False, stop=True)
                last.then_inc(y_done, 1)

            pe.wait_ge(consts_made, 1)
            turn_where(0, 0)
            with pe.Fori(0, PAIRS - 1) as p:
                for i in range(SJ):
                    look_up(p, i)
            pe.wait_ge(ident_made, 2)
            pe.wait_ge(weights_in, 16 * 5)
            pe.wait_ge(consts_made, 6)
            for i in range(len(LAST_ORDER)):
                between = {}
                if i in MLP_A:
                    between = {2: lambda: fold_sums(MLP_A[i])}
                if i in MLP_B:
                    between = {1: lambda: layer1(MLP_B[i], 0, TB), 3: lambda: layer2(MLP_B[i], 0, TB)}
                look_up(PAIRS - 1, i, LAST_ORDER, LAST_COLS, i < len(LAST_ORDER) - 1, between)
                if i in MLP_A:
                    turn_x(MLP_A[i], 0, TB)
                if i in MLP_B:
                    layer3(MLP_B[i], 0, TB)
            layer1(BLOCKS - 2, 0, TB)
            fold_sums(BLOCKS - 1)
            layer2(BLOCKS - 2, 0, TB)
            layer3(BLOCKS - 2, 0, TB)
            for m, k0, k1 in ((BLOCKS - 1, 0, TB - 1), (BLOCKS, TB - 1, TB)):
                turn_x(m, k0, k1)
                pe.wait_ge(y_made, m)
                layer1(m, k0, k1)
                layer2(m, k0, k1)
                layer3(m, k0, k1)


def kernel(r_ds_input, r_sp_input, L0_rec_emb_tables, L0_rec_lin_tables, L0_rec_lin_w, L0_rec_lin_b,
           L0_rec_w1, L0_rec_b1, L0_rec_w2, L0_rec_b2, L0_rec_fw, L0_rec_fb):
    import numpy as np
    import concourse.bacc as bacc
    from concourse.bass_utils import run_bass_kernel_spmd

    ds, sp, emb, lin, lin_w, lin_b, w1, b1, w2, b2, fw, fb = (np.asarray(a) for a in (
        r_ds_input, r_sp_input, L0_rec_emb_tables, L0_rec_lin_tables, L0_rec_lin_w, L0_rec_lin_b,
        L0_rec_w1, L0_rec_b1, L0_rec_w2, L0_rec_b2, L0_rec_fw, L0_rec_fb))
    B = sp.shape[0]
    F, C, E = emb.shape
    H1, H2 = w1.shape[0], w2.shape[0]
    P, M = 128, 6
    HIS = -(-C // (4 * P)) * 4
    zero = np.zeros((1, H1), w1.dtype)
    one = np.ones((1, 1), w1.dtype)

    def by_lo(a):
        a = np.concatenate([a, np.zeros((M, HIS * P - C, a.shape[2]), a.dtype)], axis=1)
        return a.reshape(M, HIS, P, a.shape[2]).transpose(0, 2, 1, 3).reshape(M, P, HIS * a.shape[2])

    arrays = {
        "dense": ds,
        "sparse": sp,
        "cols": np.ascontiguousarray(sp[:, :M].reshape(P, B // P, M).transpose(2, 1, 0)).reshape(M * (B // P), P),
        "table": np.concatenate([emb, lin], axis=2).reshape(F * C, E + 1),
        "tabs": np.concatenate([by_lo(emb[:M]), by_lo(lin[:M])], axis=2),
        "w1x": np.concatenate([w1.T[:E], zero, w1.T[E:], b1.reshape(1, H1), zero], axis=0),
        "w2t": np.ascontiguousarray(w2.T),
        "b2c": b2.reshape(H2, 1),
        "fwc": fw.reshape(H2, 1),
        "wlx": np.concatenate([zero.reshape(H1, 1)[:E], one, lin_w.T, lin_b.reshape(1, 1), fb.reshape(1, 1)], axis=0),
    }
    nc = bacc.Bacc("TRN2", target_bir_lowering=False, num_devices=1)
    aps = [nc.dram_tensor(n, a.shape, mybir.dt.from_np(a.dtype), kind="ExternalInput").ap()
           for n, a in arrays.items()]
    out = nc.dram_tensor("out", (ds.shape[0], 1), mybir.dt.float32, kind="ExternalOutput").ap()
    build_deep_fm(nc, *aps, out)
    return run_bass_kernel_spmd(nc, [arrays], core_ids=[0]).results[0]["out"]
```
